# Optimizing a Trainium2 kernel written in Bass

```python
import numpy as np
import jax
import jax.numpy as jnp

def _softmax(x, axis=-1):
    return jax.nn.softmax(x, axis=axis)

def _gelu(x):
    return jax.nn.gelu(x, approximate=True)

def _silu(x):
    return jax.nn.silu(x)

def _sigmoid(x):
    return jax.nn.sigmoid(x)

def _layernorm(x, axis=-1, eps=1e-05):
    m = jnp.mean(x, axis=axis, keepdims=True)
    v = jnp.var(x, axis=axis, keepdims=True)
    return (x - m) / jnp.sqrt(v + eps)

def _scatter_add(tgt, idx, src, axis=0):
    return tgt.at[idx].add(src)

def _segment_sum(src, seg, n):
    return jax.ops.segment_sum(src, seg, n)
kernel_name = 'mk_rec_standalone_d1_rec_r8_39ea29'

def setup_inputs(seed: int=0):
    np.random.seed(seed)
    _w = jnp.asarray

    def _rec_inputs():
        import jax
        import jax.numpy as jnp
        _rk = jax.random.key(seed)
        r_features = jax.random.uniform(jax.random.fold_in(_rk, 1), (512, 2, 5128), jnp.float32, 0.0, 1)
        r_stm = 0.00782532 + 1.00527 * jax.random.normal(jax.random.fold_in(_rk, 2), (512, 2, 1), jnp.float32)
        return (r_features, r_stm)
    r_features, r_stm = _rec_inputs()

    def _L0_rec_setup():
        import jax, jax.numpy as jnp
        import numpy as np
        B, P, NUM_FEATURES, M = (512, 2, 5128, 512)
        key = jax.random.key(seed)
        ks = jax.random.split(key, 8)
        return {'features': jax.random.uniform(ks[0], (B, P, NUM_FEATURES), dtype=jnp.float32), 'stm': jax.random.normal(ks[1], (B, P, 1), dtype=jnp.float32), 'W_ft': jax.random.normal(ks[2], (M, NUM_FEATURES), dtype=jnp.float32) * 0.01, 'b_ft': jax.random.normal(ks[3], (M,), dtype=jnp.float32) * 0.01, 'W1': jax.random.normal(ks[4], (32, 2 * M), dtype=jnp.float32) * 0.05, 'b1': jax.random.normal(ks[5], (32,), dtype=jnp.float32) * 0.05, 'W2': jax.random.normal(ks[6], (1, 32), dtype=jnp.float32) * 0.1, 'b2': jax.random.normal(ks[7], (1,), dtype=jnp.float32) * 0.1}
    _L0_rec_all = _L0_rec_setup()
    _L0_rec_in = {k: v for k, v in _L0_rec_all.items() if k in ('W_ft', 'b_ft', 'W1', 'b1', 'W2', 'b2')}
    del _L0_rec_all
    return {'r_features': r_features, 'r_stm': r_stm, 'L0_rec_W_ft': _L0_rec_in['W_ft'], 'L0_rec_b_ft': _L0_rec_in['b_ft'], 'L0_rec_W1': _L0_rec_in['W1'], 'L0_rec_b1': _L0_rec_in['b1'], 'L0_rec_W2': _L0_rec_in['W2'], 'L0_rec_b2': _L0_rec_in['b2']}

def reference(r_features, r_stm, L0_rec_W_ft, L0_rec_b_ft, L0_rec_W1, L0_rec_b1, L0_rec_W2, L0_rec_b2):
    import jax
    import jax.numpy as jnp

    def _L0_rec_ref(features, stm, W_ft, b_ft, W1, b1, W2, b2):
        import jax, jax.numpy as jnp
        import numpy as np
        B, P, NUM_FEATURES, M = (512, 2, 5128, 512)
        w = jnp.einsum('bpf,mf->bpm', features, W_ft) + b_ft
        accumulator = stm * w
        l1_x = jnp.clip(accumulator, 0.0, 1.0).reshape(features.shape[0], -1)
        l2_x = jnp.clip(l1_x @ W1.T + b1, 0.0, 1.0)
        return l2_x @ W2.T + b2
    y = _L0_rec_ref(r_features, r_stm, L0_rec_W_ft, L0_rec_b_ft, L0_rec_W1, L0_rec_b1, L0_rec_W2, L0_rec_b2)
    return y

_drawn_inputs = setup_inputs


def setup_inputs(seed=0):
    import zlib

    import numpy as np

    out = dict(_drawn_inputs(seed))
    spreads = {}
    factors = {'L0_rec_b_ft': 2.8}
    for name, (base, spread) in spreads.items():
        noise = np.random.default_rng([zlib.crc32(name.encode()), seed]).standard_normal(out[name].shape)
        drawn = base * np.exp(spread * noise) if base else spread * noise
        out[name] = jnp.asarray(drawn.astype(out[name].dtype))
    for name, factor in factors.items():
        out[name] = (out[name] * factor).astype(out[name].dtype)
    return out
```

```python
import concourse.bass as bass
from concourse import mybir
from contextlib import ExitStack


def feature_mlp_kernel(
    nc: bass.Bass,
    wx: bass.AP,
    b_ft: bass.AP,
    stm: bass.AP,
    w1: bass.AP,
    b1: bass.AP,
    w2b2: bass.AP,
    out: bass.AP,
):
    fp32 = mybir.dt.float32
    fp32r = mybir.dt.float32r
    ALU = mybir.AluOpType
    ACT = mybir.ActivationFunctionType

    P = 128
    F, COLS = wx.shape
    M = b_ft.shape[0] * b_ft.shape[1]
    ROWS = stm.shape[1]
    BATCH = ROWS // 2
    N = 512
    MT = M // P
    HALVES = ROWS // N
    BANKS = MT * HALVES
    H2 = w1.shape[2]
    BT = BATCH // P
    TILES = F // P
    REST = F - TILES * P
    RING = 4
    GROUPS = TILES // RING
    REST_PARTS = 3
    QUAD = 32
    assert COLS == M + ROWS and TILES == GROUPS * RING and BATCH == N and REST <= QUAD

    ctx = ExitStack()
    with ctx:
        def sb(name, shape, dt=fp32):
            return ctx.enter_context(nc.sbuf_tensor(name, shape, dt))

        def sem(name):
            return ctx.enter_context(nc.semaphore(name))

        raw = sb("raw", [P, RING, COLS])
        high = sb("high", [P, RING, COLS], fp32r)
        low = sb("low", [P, RING, COLS], fp32r)
        rest_raw = sb("rest_raw", [REST_PARTS * QUAD, COLS])
        rest = sb("rest", [REST_PARTS * QUAD, COLS], fp32r)
        b_ft_sb = sb("b_ft_sb", [P, MT])
        stm_sb = sb("stm_sb", [P, ROWS])
        w1_sb = sb("w1_sb", [P, BANKS, H2])
        b1_sb = sb("b1_sb", [1, H2])
        ones = sb("ones", [1, P])
        w2b2_sb = sb("w2b2_sb", [P, 1, H2 + 1])
        scaled = sb("scaled", [P, BANKS, N])
        l1 = sb("l1", [P, BANKS, N])
        l2 = sb("l2", [P, BT, H2 + 1])
        weighted = sb("weighted", [P, BT, H2 + 1])
        y = sb("y", [P, BT])
        acc = [ctx.enter_context(nc.psum_tensor(f"acc{b}", [P, N], fp32)) for b in range(BANKS)]
        l2_acc = acc[0][:, 0:BT * H2]

        raw_loaded = [sem(f"raw_loaded{s}") for s in range(RING)]
        first_w_loaded = sem("first_w_loaded")
        rest_cleared = sem("rest_cleared")
        rest_loaded = sem("rest_loaded")
        rest_high_ready = sem("rest_high_ready")
        rest_ready = sem("rest_ready")
        high_ready = sem("high_ready")
        low_ready = sem("low_ready")
        tile_used = sem("tile_used")
        constants_loaded = sem("constants_loaded")
        ones_ready = sem("ones_ready")
        bank_done = sem("bank_done")
        scaled_ready = sem("scaled_ready")
        l1_ready = sem("l1_ready")
        l2_done = sem("l2_done")
        l2_ready = sem("l2_ready")
        weighted_ready = sem("weighted_ready")
        y_ready = sem("y_ready")
        stored = sem("stored")

        CONSTANTS = 5
        HEAD = M + N

        def parts_of(tile):
            return tile + 2

        def tile_rows(tile):
            return wx[bass.ds(tile * P, P), :]

        block = ctx.enter_context(nc.Block())

        @block.sync
        def _(sp):
            sp.dma_start(raw[:, 0, 0:HEAD], wx[0:P, 0:HEAD]).then_inc(first_w_loaded, 16)
            sp.dma_start(raw[:, 0, HEAD:COLS], wx[0:P, HEAD:COLS]).then_inc(raw_loaded[0], 16)
            sp.wait_ge(rest_cleared, 1)
            for part in range(REST_PARTS):
                sp.dma_start(rest_raw[part * QUAD:part * QUAD + REST, :], wx[TILES * P:F, :])\
                  .then_inc(rest_loaded, 16)
            for slot in range(1, RING):
                sp.dma_start(raw[:, slot, :], tile_rows(slot)).then_inc(raw_loaded[slot], 16)
            with sp.Fori(1, GROUPS) as g:
                for slot in range(RING):
                    sp.wait_ge(low_ready, g * RING + parts_of(slot - RING))
                    sp.dma_start(raw[:, slot, :], tile_rows(g * RING + slot)).then_inc(raw_loaded[slot], 16)
            sp.wait_ge(y_ready, 1)
            sp.dma_start(out.rearrange("(p t) o -> p (t o)", t=BT), y[:, :]).then_inc(stored, 16)
            sp.wait_ge(stored, 16)

        @block.gpsimd
        def _(pool):
            pool.memset(rest_raw[:, :], 0.0).then_inc(rest_cleared, 1)
            pool.dma_start(b_ft_sb[:, :], b_ft).then_inc(constants_loaded, 16)
            pool.dma_start(stm_sb[:, :], stm.to_broadcast([P, ROWS])).then_inc(constants_loaded, 16)
            pool.dma_start(w1_sb[:, :, :], w1).then_inc(constants_loaded, 16)
            pool.dma_start(b1_sb[:, :], b1).then_inc(constants_loaded, 16)
            pool.dma_start(w2b2_sb[:, 0, :], w2b2.to_broadcast([P, H2 + 1])).then_inc(constants_loaded, 16)
            pool.memset(ones[:, :], 1.0).then_inc(ones_ready, 1)
            pool.memset(l2[:, :, H2:H2 + 1], 1.0).then_inc(ones_ready, 1)

        @block.scalar
        def _(act):
            act.wait_ge(first_w_loaded, 16)
            act.activation(high[:, 0, 0:HEAD], raw[:, 0, 0:HEAD], ACT.Copy).then_inc(high_ready, 1)
            act.wait_ge(raw_loaded[0], 16)
            act.activation(high[:, 0, HEAD:COLS], raw[:, 0, HEAD:COLS], ACT.Copy).then_inc(high_ready, 1)
            act.wait_ge(rest_loaded, 16 * REST_PARTS)
            act.activation(rest[:, :], rest_raw[:, :], ACT.Copy).then_inc(rest_high_ready, 1)
            for slot in range(1, RING):
                act.wait_ge(raw_loaded[slot], 16)
                act.activation(high[:, slot, :], raw[:, slot, :], ACT.Copy).then_inc(high_ready, 1)
            with act.Fori(1, GROUPS) as g:
                for slot in range(RING):
                    act.wait_ge(raw_loaded[slot], g * 16 + 16)
                    act.wait_ge(tile_used, g * RING + slot - RING + 1)
                    act.activation(high[:, slot, :], raw[:, slot, :], ACT.Copy).then_inc(high_ready, 1)

        @block.vector
        def _(dve):
            def split_low(slot, a, b):
                return dve.tensor_tensor(low[:, slot, a:b], raw[:, slot, a:b],
                                         high[:, slot, a:b].bitcast(fp32), ALU.subtract)

            dve.wait_ge(high_ready, 1)
            split_low(0, 0, HEAD).then_inc(low_ready, 1)
            dve.wait_ge(high_ready, 2)
            split_low(0, HEAD, COLS).then_inc(low_ready, 1)
            dve.wait_ge(rest_high_ready, 1)
            for part, a, b in ((1, 0, M), (2, M, COLS)):
                rows = slice(part * QUAD, (part + 1) * QUAD)
                dve.tensor_tensor(rest[rows, a:b], rest_raw[rows, a:b],
                                  rest[rows, a:b].bitcast(fp32), ALU.subtract).then_inc(rest_ready, 1)
            for slot in range(1, RING):
                dve.wait_ge(high_ready, parts_of(slot))
                split_low(slot, 0, COLS).then_inc(low_ready, 1)
            with dve.Fori(1, GROUPS) as g:
                for slot in range(RING):
                    dve.wait_ge(high_ready, g * RING + parts_of(slot))
                    split_low(slot, 0, COLS).then_inc(low_ready, 1)

            dve.wait_ge(constants_loaded, 16 * CONSTANTS)
            for bank in range(BANKS):
                half, m = divmod(bank, MT)
                dve.wait_ge(bank_done, bank + 1)
                dve.scalar_tensor_tensor(scaled[:, bank, :], acc[bank][:, :], b_ft_sb[:, m:m + 1],
                                         stm_sb[:, half * N:(half + 1) * N], ALU.add, ALU.mult)\
                   .then_inc(scaled_ready, 1)
                dve.wait_ge(scaled_ready, bank + 1)
                dve.tensor_scalar(l1[:, bank, :], scaled[:, bank, :], 0.0, 1.0, ALU.max, ALU.min)\
                   .then_inc(l1_ready, 1)

            dve.wait_ge(l2_done, 1)
            dve.wait_ge(ones_ready, 2)
            dve.tensor_scalar(l2[:, :, 0:H2], l2_acc.rearrange("p (t n) -> p t n", t=BT), 0.0, 1.0,
                              ALU.max, ALU.min).then_inc(l2_ready, 1)
            dve.wait_ge(l2_ready, 1)
            dve.tensor_tensor(weighted[:, :, :], l2[:, :, :], w2b2_sb[:, :, :].to_broadcast([P, BT, H2 + 1]),
                              ALU.mult).then_inc(weighted_ready, 1)
            dve.wait_ge(weighted_ready, 1)
            dve.reduce_sum(y[:, :], weighted[:, :, :], axis=mybir.AxisListType.X).then_inc(y_ready, 1)

        @block.tensor
        def _(pe):
            def product(bank, w, x, start=False, stop=False):
                half, m = divmod(bank, MT)
                return pe.matmul(acc[bank][:, :], w[:, m * P:(m + 1) * P],
                                 x[:, M + half * N:M + (half + 1) * N], start=start, stop=stop)

            def three_products(slot, bank, start=False, stop=False):
                product(bank, high[:, slot, :], high[:, slot, :], start=start)
                product(bank, high[:, slot, :], low[:, slot, :])
                return product(bank, low[:, slot, :], high[:, slot, :], stop=stop)

            def block_of_m(slot, m):
                for x in (high, low):
                    for half in range(HALVES):
                        product(half * MT + m, high[:, slot, :], x[:, slot, :])
                for half in range(HALVES):
                    last = product(half * MT + m, low[:, slot, :], high[:, slot, :])
                return last

            def feature_tile(slot):
                for m in range(MT):
                    last = block_of_m(slot, m)
                last.then_inc(tile_used, 1)

            for half in range(HALVES):
                pe.wait_ge(high_ready, half + 1)
                for m in range(MT):
                    product(half * MT + m, high[:, 0, :], high[:, 0, :], start=True)
            for half in range(HALVES):
                pe.wait_ge(low_ready, half + 1)
                for m in range(MT):
                    product(half * MT + m, high[:, 0, :], low[:, 0, :])
                    last = product(half * MT + m, low[:, 0, :], high[:, 0, :])
            last.then_inc(tile_used, 1)
            pe.wait_ge(rest_ready, 2)
            for bank in range(BANKS):
                product(bank, rest[:, :], rest[:, :])
            for slot in range(1, RING):
                pe.wait_ge(low_ready, parts_of(slot))
                feature_tile(slot)
            with pe.Fori(1, GROUPS - 1) as g:
                for slot in range(RING):
                    pe.wait_ge(low_ready, g * RING + parts_of(slot))
                    feature_tile(slot)

            def second_layer(bank):
                pe.wait_ge(l1_ready, bank + 1)
                for t in range(BT):
                    last = pe.matmul(l2_acc[:, t * H2:(t + 1) * H2], l1[:, bank, t * P:(t + 1) * P],
                                     w1_sb[:, bank, :], start=False,
                                     stop=bank == BANKS - 1 and t == BT - 1)
                return last

            for bank in range(BANKS):
                for slot in range(RING):
                    pe.wait_ge(low_ready, (GROUPS - 1) * RING + parts_of(slot))
                    last = three_products(slot, bank, stop=slot == RING - 1)
                last.then_inc(bank_done, 1)
                if bank == 1:
                    pe.wait_ge(scaled_ready, 1)
                    pe.wait_ge(ones_ready, 2)
                    pe.wait_ge(constants_loaded, 16 * CONSTANTS)
                    pe.matmul(l2_acc.rearrange("p (t n) -> p t n", t=BT), ones[:, :],
                              b1_sb[:, :].rearrange("o (t n) -> o t n", t=1).to_broadcast([1, BT, H2]),
                              start=True, stop=False)
                if bank >= 1:
                    second_layer(bank - 1)
            second_layer(BANKS - 1).then_inc(l2_done, 1)


def kernel(r_features, r_stm, L0_rec_W_ft, L0_rec_b_ft, L0_rec_W1, L0_rec_b1, L0_rec_W2, L0_rec_b2):
    import numpy as np
    import concourse.bacc as bacc
    from concourse.bass_utils import run_bass_kernel_spmd

    x, s, w_ft, b_ft, w1, b1, w2, b2 = (np.asarray(a) for a in (
        r_features, r_stm, L0_rec_W_ft, L0_rec_b_ft, L0_rec_W1, L0_rec_b1, L0_rec_W2, L0_rec_b2))
    batch, sides, features = x.shape
    m = w_ft.shape[0]
    p = 128
    t = batch // p
    x_t = x.reshape(p, t, sides, features).transpose(3, 2, 1, 0).reshape(features, sides * batch)
    stm = s.reshape(p, t, sides).transpose(2, 1, 0).reshape(1, sides * batch)
    arrays = {
        "wx": np.concatenate([w_ft.T, x_t], axis=1),
        "b_ft": b_ft.reshape(m // p, p).T,
        "stm": stm,
        "w1": w1.reshape(w1.shape[0], sides * m // p, p).transpose(2, 1, 0),
        "b1": b1.reshape(1, -1),
        "w2b2": np.concatenate([w2, b2.reshape(1, 1)], axis=1),
    }
    arrays = {name: np.ascontiguousarray(a) for name, a in arrays.items()}
    nc = bacc.Bacc("TRN2", target_bir_lowering=False, num_devices=1)
    args = [nc.dram_tensor(name, a.shape, mybir.dt.from_np(a.dtype), kind="ExternalInput").ap()
            for name, a in arrays.items()]
    out = nc.dram_tensor("y_out", (batch, 1), mybir.dt.float32, kind="ExternalOutput").ap()
    feature_mlp_kernel(nc, *args, out)
    r = run_bass_kernel_spmd(nc, [arrays], core_ids=[0])
    return r.results[0]["y_out"]
```

```python
import concourse.bass as bass
from concourse import mybir
from contextlib import ExitStack


def feature_mlp_kernel(
    nc: bass.Bass,
    wx: bass.AP,
    b_ft: bass.AP,
    stm: bass.AP,
    w1: bass.AP,
    b1: bass.AP,
    w2b2: bass.AP,
    fold: bass.AP,
    out: bass.AP,
):
    fp32 = mybir.dt.float32
    fp32r = mybir.dt.float32r
    bf16 = mybir.dt.bfloat16
    ALU = mybir.AluOpType
    ACT = mybir.ActivationFunctionType

    P = 128
    F, COLS = wx.shape
    M = b_ft.shape[0] * b_ft.shape[1]
    ROWS = stm.shape[1]
    BATCH = ROWS // 2
    N = 512
    MT = M // P
    HALVES = ROWS // N
    BANKS = MT * HALVES
    LAST = BANKS - 1
    H2 = w1.shape[2]
    BT = BATCH // P
    TILES = F // P
    REST = F - TILES * P
    RING = 5
    GROUPS = TILES // RING
    CLOSING = 4
    REST_PARTS = 3
    QUAD = 32
    WARM_UPS = 7
    W0 = N
    X0 = (0, N + M)
    assert COLS == M + ROWS and TILES == GROUPS * RING and BATCH == N and REST <= QUAD
    assert CLOSING < RING

    ctx = ExitStack()
    with ctx:
        def sb(name, shape, dt=fp32):
            return ctx.enter_context(nc.sbuf_tensor(name, shape, dt))

        def sem(name):
            return ctx.enter_context(nc.semaphore(name))

        raw = sb("raw", [P, RING, COLS])
        high = sb("high", [P, RING, COLS], fp32r)
        low = sb("low", [P, RING, COLS], fp32r)
        rest_raw = sb("rest_raw", [REST_PARTS * QUAD, COLS])
        rest = sb("rest", [REST_PARTS * QUAD, COLS], fp32r)
        warm = sb("warm", [P, 1, P], bf16)
        b_ft_sb = sb("b_ft_sb", [P, MT])
        stm_sb = sb("stm_sb", [P, ROWS])
        w1_raw = sb("w1_raw", [P, BANKS, H2])
        w1_split = sb("w1_split", [P, BANKS, P // H2, H2], fp32r)
        b1_sb = sb("b1_sb", [P, 1])
        fold_sb = sb("fold_sb", [P, H2])
        w2b2_sb = sb("w2b2_sb", [P, 1, H2 + 1])
        scaled = sb("scaled", [P, BANKS, N])
        positive = sb("positive", [P, LAST, N])
        l1_high = sb("l1_high", [P, LAST, N], fp32r)
        l1_low = sb("l1_low", [P, LAST, N], fp32r)
        l1_last = sb("l1_last", [P, N])
        l2_turned = sb("l2_turned", [P, N])
        l2 = sb("l2", [P, BT, H2 + 1])
        weighted = sb("weighted", [P, BT, H2 + 1])
        y = sb("y", [P, BT])
        acc = [ctx.enter_context(nc.psum_tensor(f"acc{b}", [P, N], fp32)) for b in range(BANKS)]
        l2_acc_turned = acc[0][:, :]
        l2_acc = acc[1][:, 0:BT * H2].rearrange("p (t n) -> p t n", t=BT)

        warm_ready = sem("warm_ready")
        raw_loaded = [sem(f"raw_loaded{s}") for s in range(RING)]
        first_x_loaded = sem("first_x_loaded")
        first_w_loaded = sem("first_w_loaded")
        first_x_high = sem("first_x_high")
        first_w_high = sem("first_w_high")
        first_low = sem("first_low")
        rest_cleared = sem("rest_cleared")
        rest_loaded = sem("rest_loaded")
        rest_high_ready = sem("rest_high_ready")
        rest_ready = sem("rest_ready")
        high_ready = sem("high_ready")
        low_ready = sem("low_ready")
        tile_used = sem("tile_used")
        constants_loaded = sem("constants_loaded")
        constants_set = sem("constants_set")
        w1_high_ready = sem("w1_high_ready")
        w1_ready = sem("w1_ready")
        bank_done = sem("bank_done")
        scaled_ready = sem("scaled_ready")
        positive_ready = sem("positive_ready")
        l1_high_ready = sem("l1_high_ready")
        l1_ready = sem("l1_ready")
        l1_last_ready = sem("l1_last_ready")
        l2_turned_done = sem("l2_turned_done")
        l2_turned_ready = sem("l2_turned_ready")
        l2_done = sem("l2_done")
        l2_ready = sem("l2_ready")
        weighted_ready = sem("weighted_ready")
        y_ready = sem("y_ready")
        stored = sem("stored")

        CONSTANTS = 6
        CONSTANTS_SET = 3

        def tile_rows(tile):
            return wx[bass.ds(tile * P, P), :]

        block = ctx.enter_context(nc.Block())

        @block.sync
        def _(sp):
            for a, b, loaded in ((X0[0], W0 + P, first_x_loaded), (W0 + P, X0[1], first_w_loaded),
                                 (X0[1], COLS, raw_loaded[0])):
                sp.dma_start(raw[:, 0, a:b], wx[0:P, a:b]).then_inc(loaded, 16)
            sp.wait_ge(rest_cleared, 1)
            for part in range(REST_PARTS):
                sp.dma_start(rest_raw[part * QUAD:part * QUAD + REST, :], wx[TILES * P:F, :])\
                  .then_inc(rest_loaded, 16)
            for slot in range(1, RING):
                sp.dma_start(raw[:, slot, :], tile_rows(slot)).then_inc(raw_loaded[slot], 16)
            with sp.Fori(1, GROUPS) as g:
                for slot in range(RING):
                    sp.wait_ge(low_ready, (g - 1) * RING + slot + 1)
                    sp.dma_start(raw[:, slot, :], tile_rows(g * RING + slot)).then_inc(raw_loaded[slot], 16)
            sp.wait_ge(y_ready, 1)
            sp.dma_start(out.rearrange("(p t) o -> p (t o)", t=BT), y[:, :]).then_inc(stored, 16)
            sp.wait_ge(stored, 16)

        @block.gpsimd
        def _(pool):
            pool.memset(rest_raw[:, :], 0.0).then_inc(rest_cleared, 1)
            pool.memset(l2[:, :, H2:H2 + 1], 1.0).then_inc(constants_set, 1)
            pool.wait_ge(low_ready, 3)
            pool.wait_ge(constants_set, CONSTANTS_SET)
            pool.dma_start(b_ft_sb[:, :], b_ft).then_inc(constants_loaded, 16)
            pool.dma_start(stm_sb[:, :], stm.to_broadcast([P, ROWS])).then_inc(constants_loaded, 16)
            pool.dma_start(w1_raw[:, :, :], w1).then_inc(constants_loaded, 16)
            pool.dma_start(b1_sb[0:H2, :], b1).then_inc(constants_loaded, 16)
            pool.dma_start(fold_sb[:, :], fold).then_inc(constants_loaded, 16)
            pool.dma_start(w2b2_sb[:, 0, :], w2b2.to_broadcast([P, H2 + 1])).then_inc(constants_loaded, 16)

        @block.scalar
        def _(act):
            def split_high(slot, a=0, b=COLS):
                return act.activation(high[:, slot, a:b], raw[:, slot, a:b], ACT.Copy)

            act.wait_ge(first_x_loaded, 16)
            split_high(0, X0[0], X0[0] + N).then_inc(first_x_high, 1)
            act.wait_ge(raw_loaded[0], 16)
            split_high(0, X0[1], X0[1] + N).then_inc(high_ready, 1)
            act.wait_ge(rest_loaded, 16 * REST_PARTS)
            act.activation(rest[:, :], rest_raw[:, :], ACT.Copy).then_inc(rest_high_ready, 1)
            for slot in range(1, RING):
                act.wait_ge(raw_loaded[slot], 16)
                split_high(slot).then_inc(high_ready, 1)
            with act.Fori(1, GROUPS) as g:
                for slot in range(RING):
                    act.wait_ge(raw_loaded[slot], g * 16 + 16)
                    act.wait_ge(tile_used, (g - 1) * RING + slot + 1)
                    split_high(slot).then_inc(high_ready, 1)

            act.wait_ge(constants_loaded, 16 * CONSTANTS)
            act.activation(w1_split[:, :, 0, :], w1_raw[:, :, :], ACT.Copy).then_inc(w1_high_ready, 1)
            for bank in range(LAST):
                act.wait_ge(scaled_ready, bank + 1)
                act.activation(positive[:, bank, :], scaled[:, bank, :], ACT.Relu).then_inc(positive_ready, 1)
            act.wait_ge(l2_turned_done, 1)
            act.wait_ge(constants_set, CONSTANTS_SET)
            for a in range(0, N, N // 2):
                act.activation(l2_turned[:, a:a + N // 2], l2_acc_turned[:, a:a + N // 2], ACT.Identity,
                               bias=b1_sb[:, :]).then_inc(l2_turned_ready, 1)

        @block.vector
        def _(dve):
            def split_low(slot, a=0, b=COLS):
                return dve.tensor_tensor(low[:, slot, a:b], raw[:, slot, a:b],
                                         high[:, slot, a:b].bitcast(fp32), ALU.subtract)

            dve.memset(warm[:, :, :], 0.0).then_inc(warm_ready, 1)
            dve.memset(b1_sb[:, :], 0.0).then_inc(constants_set, 1)
            dve.memset(w1_split[:, :, 2:, :].bitcast(fp32), 0.0).then_inc(constants_set, 1)
            dve.wait_ge(first_x_loaded, 16)
            dve.tensor_copy(high[:, 0, W0:W0 + P], raw[:, 0, W0:W0 + P]).then_inc(first_w_high, 1)
            dve.wait_ge(first_w_loaded, 16)
            dve.tensor_copy(high[:, 0, W0 + P:W0 + M], raw[:, 0, W0 + P:W0 + M]).then_inc(first_w_high, 1)
            dve.wait_ge(first_x_high, 1)
            split_low(0, X0[0], X0[0] + N).then_inc(first_low, 1)
            dve.wait_ge(first_w_high, 2)
            split_low(0, W0, W0 + M).then_inc(first_low, 1)
            dve.wait_ge(high_ready, 1)
            split_low(0, X0[1], X0[1] + N).then_inc(low_ready, 1)
            dve.wait_ge(rest_high_ready, 1)
            for part, a, b in ((1, W0, W0 + M), (2, X0[0], X0[0] + N), (2, X0[1], X0[1] + N)):
                rows = slice(part * QUAD, (part + 1) * QUAD)
                dve.tensor_tensor(rest[rows, a:b], rest_raw[rows, a:b],
                                  rest[rows, a:b].bitcast(fp32), ALU.subtract).then_inc(rest_ready, 1)
            for slot in range(1, RING):
                dve.wait_ge(high_ready, slot + 1)
                split_low(slot).then_inc(low_ready, 1)
            with dve.Fori(1, GROUPS) as g:
                for slot in range(RING):
                    dve.wait_ge(high_ready, g * RING + slot + 1)
                    split_low(slot).then_inc(low_ready, 1)

            dve.wait_ge(constants_loaded, 16 * CONSTANTS)
            dve.wait_ge(w1_high_ready, 1)
            dve.tensor_tensor(w1_split[:, :, 1, :], w1_raw[:, :, :], w1_split[:, :, 0, :].bitcast(fp32),
                              ALU.subtract).then_inc(w1_ready, 1)
            for bank in range(BANKS):
                half, m = divmod(bank, MT)
                dve.wait_ge(bank_done, bank + 1)
                dve.scalar_tensor_tensor(scaled[:, bank, :], acc[bank][:, :], b_ft_sb[:, m:m + 1],
                                         stm_sb[:, half * N:(half + 1) * N], ALU.add, ALU.mult)\
                   .then_inc(scaled_ready, 1)
                dve.wait_ge(scaled_ready, bank + 1)
                if bank == LAST:
                    continue
                dve.tensor_scalar(l1_high[:, bank, :], scaled[:, bank, :], 0.0, 1.0, ALU.max, ALU.min)\
                   .then_inc(l1_high_ready, 1)
                dve.wait_ge(positive_ready, bank + 1)
                dve.wait_ge(l1_high_ready, bank + 1)
                dve.scalar_tensor_tensor(l1_low[:, bank, :], positive[:, bank, :], 1.0,
                                         l1_high[:, bank, :].bitcast(fp32), ALU.min, ALU.subtract)\
                   .then_inc(l1_ready, 1)
            for a in range(0, N, N // 2):
                dve.tensor_scalar(l1_last[:, a:a + N // 2], scaled[:, LAST, a:a + N // 2], 0.0, 1.0,
                                  ALU.max, ALU.min).then_inc(l1_last_ready, 1)

            dve.wait_ge(l2_done, 1)
            dve.wait_ge(constants_set, CONSTANTS_SET)
            dve.tensor_scalar(l2[:, :, 0:H2], l2_acc, 0.0, 1.0, ALU.max, ALU.min).then_inc(l2_ready, 1)
            dve.wait_ge(l2_ready, 1)
            dve.tensor_tensor(weighted[:, :, :], l2[:, :, :], w2b2_sb[:, :, :].to_broadcast([P, BT, H2 + 1]),
                              ALU.mult).then_inc(weighted_ready, 1)
            dve.wait_ge(weighted_ready, 1)
            dve.reduce_sum(y[:, :], weighted[:, :, :], axis=mybir.AxisListType.X).then_inc(y_ready, 1)

        @block.tensor
        def _(pe):
            def product(bank, w, x, start=False, stop=False):
                half, m = divmod(bank, MT)
                return pe.matmul(acc[bank][:, :], w[:, W0 + m * P:W0 + (m + 1) * P],
                                 x[:, X0[half]:X0[half] + N], start=start, stop=stop)

            def feature_tile(slot):
                for m in range(MT):
                    for x in (high, low):
                        for half in range(HALVES):
                            product(half * MT + m, high[:, slot, :], x[:, slot, :])
                    for half in range(HALVES):
                        last = product(half * MT + m, low[:, slot, :], high[:, slot, :])
                return last

            pe.wait_ge(warm_ready, 1)
            for _ in range(WARM_UPS):
                pe.matmul(acc[BANKS - 1][:, :], warm[:, 0, :], warm[:, :, :].to_broadcast([P, N // P, P]),
                          start=True, stop=True)

            pe.wait_ge(first_x_high, 1)
            for m in range(MT):
                if m < 2:
                    pe.wait_ge(first_w_high, m + 1)
                product(m, high[:, 0, :], high[:, 0, :], start=True)
            pe.wait_ge(first_low, 1)
            for m in range(MT):
                product(m, high[:, 0, :], low[:, 0, :])
            pe.wait_ge(first_low, 2)
            for m in range(MT):
                product(m, low[:, 0, :], high[:, 0, :])
            pe.wait_ge(high_ready, 1)
            for m in range(MT):
                product(MT + m, high[:, 0, :], high[:, 0, :], start=True)
                product(MT + m, low[:, 0, :], high[:, 0, :])
            pe.wait_ge(low_ready, 1)
            for m in range(MT):
                last = product(MT + m, high[:, 0, :], low[:, 0, :])
            last.then_inc(tile_used, 1)
            pe.wait_ge(rest_ready, 3)
            for bank in range(BANKS):
                product(bank, rest[:, :], rest[:, :])
            for slot in range(1, RING):
                pe.wait_ge(low_ready, slot + 1)
                feature_tile(slot).then_inc(tile_used, 1)
            with pe.Fori(1, GROUPS - 1) as g:
                for slot in range(RING):
                    pe.wait_ge(low_ready, g * RING + slot + 1)
                    feature_tile(slot).then_inc(tile_used, 1)
            for slot in range(RING - CLOSING):
                pe.wait_ge(low_ready, (GROUPS - 1) * RING + slot + 1)
                feature_tile(slot).then_inc(tile_used, 1)

            def second_layer(bank, l1, ready):
                pe.wait_ge(ready, bank + 1)
                return pe.matmul(l2_acc_turned, w1_split[:, bank, :, :].rearrange("p s n -> p (s n)"),
                                 l1[:, bank, :], start=bank == 0 and l1 is l1_high,
                                 stop=bank == LAST - 1 and l1 is l1_low)

            for bank in range(BANKS):
                for slot in range(RING - CLOSING, RING):
                    if bank == 0:
                        pe.wait_ge(low_ready, (GROUPS - 1) * RING + slot + 1)
                    follows = bank >= 1 and slot == RING - 1
                    if follows:
                        if bank == 1:
                            pe.wait_ge(w1_ready, 1)
                            pe.wait_ge(constants_set, CONSTANTS_SET)
                        second_layer(bank - 1, l1_high, l1_high_ready)
                    product(bank, high[:, slot, :], high[:, slot, :])
                    if bank < LAST:
                        product(bank, high[:, slot, :], low[:, slot, :])
                    if follows:
                        turned = second_layer(bank - 1, l1_low, l1_ready)
                        if bank == LAST:
                            turned.then_inc(l2_turned_done, 1)
                    if bank == LAST:
                        product(bank, high[:, slot, :], low[:, slot, :])
                    last = product(bank, low[:, slot, :], high[:, slot, :], stop=slot == RING - 1)
                last.then_inc(bank_done, 1)

            pe.wait_ge(constants_loaded, 16 * CONSTANTS)
            for t in range(BT):
                if t % (BT // 2) == 0:
                    pe.wait_ge(l2_turned_ready, 2 * t // BT + 1)
                pe.matmul(l2_acc[:, t, :], l2_turned[:, t * P:(t + 1) * P], fold_sb[:, :], start=t == 0, stop=False)
            for t in range(BT):
                if t % (BT // 2) == 0:
                    pe.wait_ge(l1_last_ready, 2 * t // BT + 1)
                last = pe.matmul(l2_acc[:, t, :], l1_last[:, t * P:(t + 1) * P], w1_raw[:, LAST, :],
                                 start=False, stop=t == BT - 1)
            last.then_inc(l2_done, 1)


def kernel(r_features, r_stm, L0_rec_W_ft, L0_rec_b_ft, L0_rec_W1, L0_rec_b1, L0_rec_W2, L0_rec_b2):
    import numpy as np
    import concourse.bacc as bacc
    from concourse.bass_utils import run_bass_kernel_spmd

    x, s, w_ft, b_ft, w1, b1, w2, b2 = (np.asarray(a) for a in (
        r_features, r_stm, L0_rec_W_ft, L0_rec_b_ft, L0_rec_W1, L0_rec_b1, L0_rec_W2, L0_rec_b2))
    batch, sides, features = x.shape
    m = w_ft.shape[0]
    p = 128
    t = batch // p
    x_t = x.reshape(p, t, sides, features).transpose(3, 2, 1, 0).reshape(features, sides * batch)
    stm = s.reshape(p, t, sides).transpose(2, 1, 0).reshape(1, sides * batch)
    arrays = {
        "wx": np.concatenate([x_t[:, :batch], w_ft.T, x_t[:, batch:]], axis=1),
        "b_ft": b_ft.reshape(m // p, p).T,
        "stm": stm,
        "w1": w1.reshape(w1.shape[0], sides * m // p, p).transpose(2, 1, 0),
        "b1": b1.reshape(-1, 1),
        "w2b2": np.concatenate([w2, b2.reshape(1, 1)], axis=1),
        "fold": np.eye(p, w1.shape[0], dtype=np.float32) + np.eye(p, w1.shape[0], -w1.shape[0], dtype=np.float32),
    }
    arrays = {name: np.ascontiguousarray(a) for name, a in arrays.items()}
    nc = bacc.Bacc("TRN2", target_bir_lowering=False, num_devices=1)
    args = [nc.dram_tensor(name, a.shape, mybir.dt.from_np(a.dtype), kind="ExternalInput").ap()
            for name, a in arrays.items()]
    out = nc.dram_tensor("y_out", (batch, 1), mybir.dt.float32, kind="ExternalOutput").ap()
    feature_mlp_kernel(nc, *args, out)
    r = run_bass_kernel_spmd(nc, [arrays], core_ids=[0])
    return r.results[0]["y_out"]
```
